# Optimizing a Trainium2 kernel written in Bass

```python
import numpy as np
import jax
import jax.numpy as jnp

def _softmax(x, axis=-1):
    return jax.nn.softmax(x, axis=axis)

def _gelu(x):
    return jax.nn.gelu(x, approximate=True)

def _silu(x):
    return jax.nn.silu(x)

def _sigmoid(x):
    return jax.nn.sigmoid(x)

def _layernorm(x, axis=-1, eps=1e-05):
    m = jnp.mean(x, axis=axis, keepdims=True)
    v = jnp.var(x, axis=axis, keepdims=True)
    return (x - m) / jnp.sqrt(v + eps)

def _scatter_add(tgt, idx, src, axis=0):
    return tgt.at[idx].add(src)

def _segment_sum(src, seg, n):
    return jax.ops.segment_sum(src, seg, n)
kernel_name = 'mk_gnn_preln_d4_gnn_r32_4e2805'

def setup_inputs(seed: int=0):
    np.random.seed(seed)
    _w = jnp.asarray

    def _rec_inputs():
        import jax
        import jax.numpy as jnp
        _gk = jax.random.key(seed)
        x = -0.0003713 + 1 * jax.random.normal(jax.random.fold_in(_gk, 1), (3125, 256), jnp.float32)
        src = jax.random.randint(jax.random.fold_in(_gk, 2), (50000,), 0, 3125, jnp.int32)
        dst = jax.random.randint(jax.random.fold_in(_gk, 3), (50000,), 0, 3125, jnp.int32)
        _o = jnp.argsort(dst, stable=True)
        src = src[_o]
        dst = dst[_o]
        edge_attr_3 = -1.09012e-05 + 0.99985 * jax.random.normal(jax.random.fold_in(_gk, 12), (50000, 3), jnp.float32)
        edge_type_32 = jax.random.randint(jax.random.fold_in(_gk, 14), (50000,), 0, 32, jnp.int32)
        edge_weight1 = jax.random.uniform(jax.random.fold_in(_gk, 15), (50000, 1), jnp.float32, 0.0, 0.999998)
        return (x, src, dst, edge_attr_3, edge_type_32, edge_weight1)
    x, src, dst, edge_attr_3, edge_type_32, edge_weight1 = _rec_inputs()

    def _L0_gnn_setup():
        import jax, jax.numpy as jnp
        import numpy as np
        N = 50000
        E = 25000
        DIM = 256
        H = 8
        DH = DIM // H
        SCALE = DH ** (-0.5)
        key = jax.random.key(seed)
        ks = jax.random.split(key, 7)
        h = jax.random.normal(ks[0], (N, DIM), dtype=jnp.float32)
        src = jax.random.randint(ks[1], (E,), 0, N, dtype=jnp.int32)
        dst = jax.random.randint(ks[2], (E,), 0, N, dtype=jnp.int32)
        W_qkv = jax.random.normal(ks[3], (DIM, 3 * DIM), dtype=jnp.float32) * DIM ** (-0.5)
        b_qkv = jnp.zeros((3 * DIM,), dtype=jnp.float32)
        W_out = jax.random.normal(ks[4], (DIM, DIM), dtype=jnp.float32) * DIM ** (-0.5)
        b_out = jnp.zeros((DIM,), dtype=jnp.float32)
        return {'h': h, 'src': src, 'dst': dst, 'W_qkv': W_qkv, 'b_qkv': b_qkv, 'W_out': W_out, 'b_out': b_out}
    _L0_gnn_all = _L0_gnn_setup()
    _L0_gnn_in = {k: v for k, v in _L0_gnn_all.items() if k in ('W_qkv', 'b_qkv', 'W_out', 'b_out')}
    del _L0_gnn_all

    def _L1_gnn_setup():
        import jax, jax.numpy as jnp
        import numpy as np
        N = 50000
        E = 12500
        IN = 256
        H = 8
        D = 32
        EF = 3
        key = jax.random.key(seed)
        ks = jax.random.split(key, 8)
        x = jax.random.normal(ks[0], (N, IN), dtype=jnp.float32)
        edge_index = jax.random.randint(ks[1], (2, E), 0, N, dtype=jnp.int64)
        edge_attr = jax.random.normal(ks[2], (E, EF), dtype=jnp.float32)
        W = jax.random.normal(ks[3], (H * D, IN), dtype=jnp.float32) * np.float32(np.sqrt(2.0 / (IN + H * D)))
        a_src = jax.random.normal(ks[4], (H, D), dtype=jnp.float32) * np.float32(np.sqrt(2.0 / (H + D)))
        a_dst = jax.random.normal(ks[5], (H, D), dtype=jnp.float32) * np.float32(np.sqrt(2.0 / (H + D)))
        edge_W = jax.random.normal(ks[6], (H * D, EF), dtype=jnp.float32) * np.float32(np.sqrt(2.0 / (EF + H * D)))
        edge_b = jnp.zeros((H * D,), dtype=jnp.float32)
        bias = jnp.zeros((H * D,), dtype=jnp.float32)
        return {'x': x, 'W': W, 'a_src': a_src, 'a_dst': a_dst, 'edge_W': edge_W, 'edge_b': edge_b, 'bias': bias, 'edge_attr': edge_attr, 'edge_index': edge_index}
    _L1_gnn_all = _L1_gnn_setup()
    _L1_gnn_in = {k: v for k, v in _L1_gnn_all.items() if k in ('W', 'a_src', 'a_dst', 'edge_W', 'edge_b', 'bias')}
    del _L1_gnn_all

    def _L2_gnn_setup():
        import jax, jax.numpy as jnp
        import numpy as np
        N, IN_CH, HEADS, OUT_CH, E = (50000, 256, 4, 64, 25000)
        key = jax.random.key(seed)
        k1, k2, k3, k4, k5 = jax.random.split(key, 5)
        x = jax.random.normal(k1, (N, IN_CH), dtype=jnp.float32)
        edge_index = jax.random.randint(k2, (2, E), 0, N, dtype=jnp.int64)
        bw = float(np.sqrt(6.0 / (IN_CH + HEADS * OUT_CH)))
        ba = float(np.sqrt(6.0 / (HEADS + OUT_CH)))
        weight = jax.random.uniform(k3, (IN_CH, HEADS * OUT_CH), jnp.float32, -bw, bw)
        attn_l = jax.random.uniform(k4, (HEADS, OUT_CH), jnp.float32, -ba, ba)
        attn_r = jax.random.uniform(k5, (HEADS, OUT_CH), jnp.float32, -ba, ba)
        return {'x': x, 'edge_index': edge_index, 'weight': weight, 'attn_l': attn_l, 'attn_r': attn_r}
    _L2_gnn_all = _L2_gnn_setup()
    _L2_gnn_in = {k: v for k, v in _L2_gnn_all.items() if k in ('weight', 'attn_l', 'attn_r')}
    del _L2_gnn_all

    def _L3_gnn_setup():
        import jax, jax.numpy as jnp
        import numpy as np
        N_NODES = 625
        N_EDGES = 10000
        IN_DIM = 256
        OUT_DIM = 256
        NUM_RELS = 32
        NUM_BASES = 8
        key = jax.random.key(seed)
        k1, k2, k3, k4, k5, k6, k7 = jax.random.split(key, 7)
        h = jax.random.normal(k1, (N_NODES, IN_DIM), dtype=jnp.float32)
        src = jax.random.randint(k2, (N_EDGES,), 0, N_NODES, dtype=jnp.int32)
        dst = jax.random.randint(k3, (N_EDGES,), 0, N_NODES, dtype=jnp.int32)
        rel_type = jax.random.randint(k4, (N_EDGES,), 0, NUM_RELS, dtype=jnp.int32)
        norm = jax.random.uniform(k5, (N_EDGES, 1), dtype=jnp.float32)
        scale_w = np.sqrt(2.0) * np.sqrt(6.0 / (IN_DIM + OUT_DIM))
        bases = jax.random.uniform(k6, (NUM_BASES, IN_DIM, OUT_DIM), dtype=jnp.float32, minval=-scale_w, maxval=scale_w)
        scale_c = np.sqrt(2.0) * np.sqrt(6.0 / (NUM_RELS + NUM_BASES))
        w_comp = jax.random.uniform(k7, (NUM_RELS, NUM_BASES), dtype=jnp.float32, minval=-scale_c, maxval=scale_c)
        return {'h': h, 'src': src, 'dst': dst, 'rel_type': rel_type, 'norm': norm, 'bases': bases, 'w_comp': w_comp}
    _L3_gnn_all = _L3_gnn_setup()
    _L3_gnn_in = {k: v for k, v in _L3_gnn_all.items() if k in ('bases', 'w_comp')}
    del _L3_gnn_all
    return {'x': x, 'src': src, 'dst': dst, 'edge_attr_3': edge_attr_3, 'edge_type_32': edge_type_32, 'edge_weight1': edge_weight1, 'L0_gnn_W_qkv': _L0_gnn_in['W_qkv'], 'L0_gnn_b_qkv': _L0_gnn_in['b_qkv'], 'L0_gnn_W_out': _L0_gnn_in['W_out'], 'L0_gnn_b_out': _L0_gnn_in['b_out'], 'L1_gnn_W': _L1_gnn_in['W'], 'L1_gnn_a_src': _L1_gnn_in['a_src'], 'L1_gnn_a_dst': _L1_gnn_in['a_dst'], 'L1_gnn_edge_W': _L1_gnn_in['edge_W'], 'L1_gnn_edge_b': _L1_gnn_in['edge_b'], 'L1_gnn_bias': _L1_gnn_in['bias'], 'L2_gnn_weight': _L2_gnn_in['weight'], 'L2_gnn_attn_l': _L2_gnn_in['attn_l'], 'L2_gnn_attn_r': _L2_gnn_in['attn_r'], 'L3_gnn_bases': _L3_gnn_in['bases'], 'L3_gnn_w_comp': _L3_gnn_in['w_comp']}

def reference(x, src, dst, edge_attr_3, edge_type_32, edge_weight1, L0_gnn_W_qkv, L0_gnn_b_qkv, L0_gnn_W_out, L0_gnn_b_out, L1_gnn_W, L1_gnn_a_src, L1_gnn_a_dst, L1_gnn_edge_W, L1_gnn_edge_b, L1_gnn_bias, L2_gnn_weight, L2_gnn_attn_l, L2_gnn_attn_r, L3_gnn_bases, L3_gnn_w_comp):
    import jax
    import jax.numpy as jnp

    def _L0_gnn_ref(h, src, dst, W_qkv, b_qkv, W_out, b_out):
        import jax, jax.numpy as jnp
        import numpy as np
        N = 50000
        E = 25000
        DIM = 256
        H = 8
        DH = DIM // H
        SCALE = DH ** (-0.5)
        n = h.shape[0]
        qkv = (h @ W_qkv + b_qkv).reshape(n, 3, H, DH)
        q, k, v = (qkv[:, 0], qkv[:, 1], qkv[:, 2])
        score = jnp.einsum('ehd,ehd->eh', q[dst], k[src]) * SCALE
        mx = jax.ops.segment_max(score, dst, num_segments=n)
        ex = jnp.exp(score - mx[dst])
        denom = jax.ops.segment_sum(ex, dst, num_segments=n)
        attn = ex / denom[dst]
        msg = attn[:, :, None] * v[src]
        h_new = jax.ops.segment_sum(msg, dst, num_segments=n)
        h_out = jnp.transpose(h_new, (0, 2, 1)).reshape(n, DIM)
        return (h_out + h) @ W_out + b_out

    def _L1_gnn_ref(x, W, a_src, a_dst, edge_W, edge_b, bias, edge_attr, edge_index):
        import jax, jax.numpy as jnp
        import numpy as np
        N = 50000
        E = 12500
        IN = 256
        H = 8
        D = 32
        EF = 3
        n = x.shape[0]
        h = (x @ W.T).reshape(n, H, D)
        src, dst = (edge_index[0], edge_index[1])
        h_src = h[src]
        h_dst = h[dst]
        alpha = jnp.einsum('ehd,hd->eh', h_src, a_src) + jnp.einsum('ehd,hd->eh', h_dst, a_dst)
        enc = jax.nn.relu(edge_attr @ edge_W.T + edge_b).reshape(-1, H, D)
        alpha = alpha + jnp.sum(enc * h_dst, axis=-1)
        alpha = jnp.where(alpha >= 0, alpha, 0.2 * alpha)
        amax = jax.ops.segment_max(alpha, dst, num_segments=n)
        ex = jnp.exp(alpha - amax[dst])
        denom = jax.ops.segment_sum(ex, dst, num_segments=n)
        attn = ex / jnp.maximum(denom[dst], 1e-10)
        out = jax.ops.segment_sum(h_src * attn[..., None], dst, num_segments=n)
        return out.reshape(n, H * D) + bias

    def _L2_gnn_ref(x, edge_index, weight, attn_l, attn_r):
        import jax, jax.numpy as jnp
        import numpy as np
        N, IN_CH, HEADS, OUT_CH, E = (50000, 256, 4, 64, 25000)
        heads, out_ch = attn_l.shape
        n = x.shape[0]
        xt = jnp.matmul(x, weight).reshape(-1, heads, out_ch)
        row, col = (edge_index[0], edge_index[1])
        alpha_l = jnp.einsum('ehd,hd->eh', xt[row], attn_l)
        alpha_r = jnp.einsum('ehd,hd->eh', xt[col], attn_r)
        alpha = jax.nn.softmax(jax.nn.leaky_relu(alpha_l + alpha_r, 0.01), axis=1)
        tmp = jnp.einsum('nh,nhd->nd', alpha[:n], xt[col[:n]])
        out = jnp.broadcast_to(tmp[:, None, :], (n, heads, out_ch))
        return out.reshape(n, heads * out_ch)

    def _L3_gnn_ref(h, src, dst, rel_type, norm, bases, w_comp):
        import jax, jax.numpy as jnp
        import numpy as np
        N_NODES = 625
        N_EDGES = 10000
        IN_DIM = 256
        OUT_DIM = 256
        NUM_RELS = 32
        NUM_BASES = 8
        weight = jnp.einsum('rb,bio->rio', w_comp, bases)
        xw = jnp.einsum('ni,rio->nro', h, weight)
        msg = xw[src, rel_type] * norm
        out = jax.ops.segment_sum(msg, dst, num_segments=h.shape[0])
        return jax.nn.relu(out)
    edge_index = jnp.stack([src, dst])
    h = jnp.maximum(_layernorm(x, axis=-1), 0.0)
    x = x + _L0_gnn_ref(h, src, dst, L0_gnn_W_qkv, L0_gnn_b_qkv, L0_gnn_W_out, L0_gnn_b_out)
    h = jnp.maximum(_layernorm(x, axis=-1), 0.0)
    x = x + _L1_gnn_ref(h, L1_gnn_W, L1_gnn_a_src, L1_gnn_a_dst, L1_gnn_edge_W, L1_gnn_edge_b, L1_gnn_bias, edge_attr_3, edge_index)
    h = jnp.maximum(_layernorm(x, axis=-1), 0.0)
    x = x + _L2_gnn_ref(h, edge_index, L2_gnn_weight, L2_gnn_attn_l, L2_gnn_attn_r)
    h = jnp.maximum(_layernorm(x, axis=-1), 0.0)
    x = x + _L3_gnn_ref(h, src, dst, edge_type_32, edge_weight1, L3_gnn_bases, L3_gnn_w_comp)
    return x

_drawn_inputs = setup_inputs


def setup_inputs(seed=0):
    import zlib

    import numpy as np

    out = dict(_drawn_inputs(seed))
    spreads = {'L0_gnn_b_qkv': (0.0, 0.1),
     'L0_gnn_b_out': (0.0, 0.1),
     'L1_gnn_edge_b': (0.0, 0.557),
     'L1_gnn_bias': (0.0, 0.1)}
    factors = {'L1_gnn_a_dst': 2.866}
    for name, (base, spread) in spreads.items():
        noise = np.random.default_rng([zlib.crc32(name.encode()), seed]).standard_normal(out[name].shape)
        drawn = base * np.exp(spread * noise) if base else spread * noise
        out[name] = jnp.asarray(drawn.astype(out[name].dtype))
    for name, factor in factors.items():
        out[name] = (out[name] * factor).astype(out[name].dtype)
    return out
```

```python
from contextlib import ExitStack

import concourse.bass as bass
from concourse import mybir

F32 = mybir.dt.float32
BF16 = mybir.dt.bfloat16
I32 = mybir.dt.int32
ALU = mybir.AluOpType
ACT = mybir.ActivationFunctionType
AX = mybir.AxisListType

P = 128
N, D, E = 3125, 256, 50000
TP = 125
NT = N // TP
KC = D // P
H = 8
H2 = 4
R, B = 32, 8
EPS = 1e-5
U = 16
HALF = U // 2
STEPS = -(-(E + NT * (P - 1)) // P)
STEPS = -(-STEPS // U) * U
ROUNDS = STEPS // U
GRP = -(-STEPS // P)
EW = 400
EP = E // EW
UT = 5
TR = NT // UT
W1 = D + H
JS = 2 * U
CH = STEPS // JS
RW = CH * H
NB = JS // 4
RL = JS * P
NEG = -1.0e30
FAR = 1.0e6
REC = 8
OHB = 8
MB = 4
XC = 2048
CREDIT = 96
assert RW <= P and STEPS == JS * CH and NT == UT * TR


def build(nc, x, src, dst, attr, etype, weight, w_qkv, b_qkv, w_out, b_out, w1, w1t, a_src, a_dst, edge_wt,
          edge_b, bias1, w2, w2t, attn_l, attn_r, bases, w_comp, out):
    with ExitStack() as ctx:
        ctx.enter_context(nc.allow_non_contiguous_dma(reason="a few small index and vector loads"))

        def sb(name, shape, dt=F32):
            return ctx.enter_context(nc.sbuf_tensor(name, shape, dt))

        def sem(name):
            return ctx.enter_context(nc.semaphore(name))

        def dram(name, shape, dt=F32):
            return nc.dram_tensor(name, shape, dt, kind="Internal").ap()

        rec_tab = dram("rec_tab", (E + P, REC))
        step_tab = dram("step_tab", (2, GRP * P), I32)
        k_tab = dram("k_tab", (N, D))
        v_tab = dram("v_tab", (N, D))
        hw_tab = dram("hw_tab", (N, D))
        ss_tab = dram("ss_tab", (N, H))
        xt_tab = dram("xt_tab", (N, W1))
        sl_tab = dram("sl_tab", (N, H2))
        xw_tab = dram("xw_tab", (N * R, D))

        X = sb("X", [P, NT, D])
        UNI = sb("UNI", [P, max(2 * RL, 4 * XC)])
        QTN, SCN = NT * W1, STEPS * H
        BIG = sb("BIG", [P, max(R * D * KC, QTN + 2 * SCN + RL // 2 + 64)])
        recs = sb("recs", [P, STEPS, REC])
        ring = sb("ring", [P, U, D])
        QT = BIG[:, 0:QTN].rearrange("p (t c) -> p t c", c=W1)
        SC = BIG[:, QTN:QTN + SCN].rearrange("p (s h) -> p s h", h=H)
        SS = BIG[:, QTN + SCN:QTN + 2 * SCN].rearrange("p (s h) -> p s h", h=H)
        penN = QTN + 2 * SCN
        PEN = BIG[0:RW, penN:penN + RL // 2 + 32].bitcast(BF16)
        lineN = penN + RL // 2 + 32
        line_ = BIG[0:1, lineN:lineN + 10 * RW].rearrange("p (a b) -> p a b", b=RW)
        VST = BIG[:, QTN:QTN + NT * D].rearrange("p (t c) -> p t c", c=D)
        KST = UNI[:, 0:NT * D].rearrange("p (t c) -> p t c", c=D)
        ACC = UNI[:, 0:QTN].rearrange("p (t c) -> p t c", c=W1)
        RS = UNI[0:RW, 0:RL]
        RF = UNI[0:RW, RL:2 * RL]
        KR = RS
        RM = BIG[0:RW, QTN:QTN + RL]
        resid = ring[:, 0:UT, :]
        WR = BIG[:, 0:KC * R * D].rearrange("p (c r o) -> p c r o", c=KC, r=R)
        BASES = ring[:, :, :].rearrange("p (b c) o -> p b c o", c=KC)
        xst = [UNI[:, q * XC:(q + 1) * XC] for q in range(4)]
        Hb = ring[:, UT:2 * UT, :]
        HT = ring[:, 2 * UT:3 * UT, :].rearrange("p k (c n) -> p k c n", c=KC)
        at = [0]

        def scratch(n):
            at[0] += n
            return BIG[:, at[0] - n:at[0]]
        dstI, srcI, typI = (scratch(EW)[0:EP].bitcast(I32) for _ in range(3))
        wF, atF = scratch(EW)[0:EP], scratch(3 * EW)[0:EP].rearrange("p (e a) -> p e a", a=3)
        recF = scratch(REC * EW)[0:EP].rearrange("p (e r) -> p e r", r=REC)
        junk = scratch(EW)[0:EP]
        padrec = scratch(REC)
        oh = sb("oh", [P, OHB, P])
        ohT = sb("ohT", [P, 2, P])
        enc = sb("enc", [P, 2, D])
        prod = sb("prod", [P, 2, D])
        msg = sb("msg", [P, MB, D])
        wqkv = sb("wqkv", [P, KC, 3 * D])
        bqkv = sb("bqkv", [1, 3 * D])
        wout = sb("wout", [P, KC, D])
        bout = sb("bout", [1, D])
        w1c = sb("w1c", [P, KC, D + 2 * H])
        w1n = msg[:, 0:KC, :]
        a1 = sb("a1", [P, KC, 2 * H])
        w2c = sb("w2c", [P, KC, D + 2 * H2])
        w2n = msg[:, KC:2 * KC, :]
        a2 = sb("a2", [P, KC, 2 * H2])
        encw = sb("encw", [P, D])
        bias1b = sb("bias1b", [P, D])
        wcb = sb("wcb", [P, R * B])
        ident = sb("ident", [P, P])
        nodeI = sb("nodeI", [P, TP], I32)
        node = sb("node", [P, TP])
        ones = sb("ones", [P, P])
        dloc = sb("dloc", [P, STEPS])
        key = sb("key", [P, STEPS])
        idx = sb("idx", [P, STEPS], I32)
        idx3 = sb("idx3", [P, STEPS], I32)
        blkb = sb("blkb", [P, STEPS], I32)
        stage = sb("stage", [P, 2, HALF], I32)
        rows = sb("rows", [1, 2, GRP * P], I32)
        colI, rowI = sb("colI", [P, NT], I32), sb("rowI", [P, NT], I32)
        cnt = sb("cnt", [P, NT])
        first = sb("first", [P, NT + 1])
        ne, ns, nsI, cum, gap, mask = (sb(n, [P, NT], I32 if n == "nsI" else F32)
                                       for n in ("ne", "ns", "nsI", "cum", "gap", "mask"))
        gridI, grid, blkF, estF = (sb(n, [P, GRP], I32 if n == "gridI" else F32)
                                   for n in ("gridI", "grid", "blkF", "estF"))
        tabI = sb("tabI", [P, 2, GRP], I32)
        st6 = sb("st6", [P, NT, 6])
        lnw = sb("lnw", [P, 3, NT])
        std, rstd, nmr = (sb(n, [P, NT]) for n in ("std", "rstd", "nmr"))
        SL8 = sb("SL8", [P, NT, H])
        edge = sb("edge", [RW, 4])
        init = sb("init", [RW, 2])
        s2 = sb("s2", [P, NT, H2])
        m2 = sb("m2", [P, 2, NT])
        o2 = BIG[:, QTN:QTN + NT * D // H2].rearrange("p (t d) -> p t d", d=D // H2)
        SL = sb("SL", [P, NT, H2])

        bank = [ctx.enter_context(nc.psum_tensor(f"bank{i}", [P, 512], F32)) for i in range(8)]
        tr, mm, ag = bank[0:2], bank[2:6], bank[6:8]

        ld_edge, ld_w, ld_x, ld_b2 = sem("ld_edge"), sem("ld_w"), sem("ld_x"), sem("ld_b2")
        const_ready, diag_zero, diag_ready = sem("const_ready"), sem("diag_zero"), sem("diag_ready")
        rec_built, rec_stored, cnt_ready, first_ps = sem("rec_built"), sem("rec_stored"), sem("cnt_ready"), sem("first_ps")
        steps_ready, steps_stored, steps_back, recs_in = (sem("steps_ready"), sem("steps_stored"),
                                                           sem("steps_back"), sem("recs_in"))
        idx_ready, key_ps, key_copied = sem("idx_ready"), sem("key_ps"), sem("key_copied")
        edge_ready, edge_ps, line_ready, init_ps = sem("edge_ready"), sem("edge_ps"), sem("line_ready"), sem("init_ps")
        line_in = sem("line_in")
        wa_ps, wa_ready = sem("wa_ps"), sem("wa_ready")
        dve_line, act_line, pool_line = sem("dve_line"), sem("act_line"), sem("pool_line")
        bn_s, var_ready, std_ready, ln_ready = (sem("bn_s"), sem("var_ready"),
                                                      sem("std_ready"), sem("ln_ready"))
        h_ready, hT_ps, hT_copied, mm_done, ev_act, ev_dve = (sem("h_ready"), sem("hT_ps"), sem("hT_copied"),
                                                              sem("mm_done"), sem("ev_act"), sem("ev_dve"))
        pre_h, pre_u, pre_d, x_done = sem("pre_h"), sem("pre_u"), sem("pre_d"), sem("x_done")
        tab_stored = sem("tab_stored")
        staged = sem("staged")
        got = [sem(f"got{k}") for k in range(U)]
        oh_ready, ohT_ps, ohT_copied, qd_ready = sem("oh_ready"), sem("ohT_ps"), sem("ohT_copied"), sem("qd_ready")
        attr_in, enc_ps, enc_copied, ss_copied = sem("attr_in"), sem("enc_ps"), sem("enc_copied"), sem("ss_copied")
        prod_ready, score_ready, sdst_added = sem("prod_ready"), sem("score_ready"), sem("sdst_added")
        sc_final, row_ps, row_copied, row_exp, col_ps, ex_ready = (sem("sc_final"), sem("row_ps"), sem("row_copied"),
                                                                   sem("row_exp"), sem("col_ps"), sem("ex_ready"))
        rows_shifted = sem("rows_shifted")
        msg_ready, agg_ready, acc_done = sem("msg_ready"), sem("agg_ready"), sem("acc_done")
        edge_rows, wr_ready = sem("edge_rows"), sem("wr_ready")
        xw_ps, xw_copied_a, xw_copied_v = sem("xw_ps"), sem("xw_copied_a"), sem("xw_copied_v")
        xst_free = [sem(f"xst_free{q}") for q in range(4)]
        x_final, out_stored = sem("x_final"), sem("out_stored")
        PE_PACED = (hT_ps, mm_done, ohT_ps, qd_ready, enc_ps, agg_ready, row_ps, col_ps, xw_ps, key_ps)
        ACT_PACED = (h_ready, ohT_copied, enc_copied, ss_copied, ev_act, xw_copied_a, attr_in)
        DVE_PACED = (hT_copied, prod_ready, score_ready, msg_ready, acc_done, ev_dve, xw_copied_v, oh_ready,
                     bn_s, pre_u, pre_d, x_done, sdst_added, row_copied)
        C = CREDIT

        QKV, POST0, LIN1, LIN2, XW = range(5)
        A0, B0, A1, B1, B3 = range(5)

        NOTE_T = "blocks are counted from the step number and never pass NT - 1"
        NOTE_E = "first edges are clamped to E, and the record table has P rows more"

        def round_blocks(engine_type, i):
            return nc.values_load_multi_w_load_instructions(
                rows[0:1, 0, bass.ds(i * U, U)], engines=[engine_type], min_val=0, max_val=NT - 1,
                skip_runtime_bounds_check_because=NOTE_T)[1]

        def place(i, k):
            if not isinstance(i, int):
                return (i % 2) * (U * CH) + (i >> 1) + k * CH
            return (i % 2) * (U * CH) + i // 2 + k * CH

        def rounds(eng, body):
            with eng.Fori(0, ROUNDS - 1) as i:
                body(i, False)
            body(ROUNDS - 1, True)

        block = ctx.enter_context(nc.Block())

        @block.sync
        def _(sp):
            for t, a in ((dstI, dst), (srcI, src), (typI, etype)):
                sp.dma_start(t, a.rearrange("(p e) -> p e", e=EW)).then_inc(ld_edge, 16)
            sp.dma_start(wF, weight.rearrange("(p e) a -> p (e a)", e=EW)).then_inc(ld_edge, 16)
            sp.dma_start(atF, attr.rearrange("(p e) a -> p e a", e=EW)).then_inc(ld_edge, 16)
            sp.dma_start(X[0:TP], x.rearrange("(t p) d -> p t d", p=TP)).then_inc(ld_x, 16)
            for t, a in ((wqkv, w_qkv), (wout, w_out), (w1n, w1), (w2n, w2t)):
                sp.dma_start(t[:, :, :], a.rearrange("(c p) n -> p c n", p=P)).then_inc(ld_w, 16)
            sp.dma_start(w1c[:, :, 0:D], w1t.rearrange("(c p) n -> p c n", p=P)).then_inc(ld_w, 16)
            sp.dma_start(w2c[:, :, 0:D], w2.rearrange("(c p) n -> p c n", p=P)).then_inc(ld_w, 16)
            sp.dma_start(bqkv[:, :], b_qkv.rearrange("(a n) -> a n", a=1)).then_inc(ld_w, 16)
            sp.dma_start(bout[:, :], b_out.rearrange("(a n) -> a n", a=1)).then_inc(ld_w, 16)
            sp.dma_start(encw[0:TP, :], edge_b.partition_broadcast(TP)).then_inc(ld_w, 16)
            sp.dma_start(encw[TP:P, :], edge_wt).then_inc(ld_w, 16)
            sp.dma_start(bias1b[:, :], bias1.partition_broadcast(P)).then_inc(ld_w, 16)
            sp.dma_start(wcb[:, :], w_comp.rearrange("r b -> (r b)").partition_broadcast(P)).then_inc(ld_w, 16)
            sp.dma_start(colI[0:TP, :], dst[0:N].rearrange("(t p) -> p t", p=TP)).then_inc(ld_w, 16)
            sp.dma_start(rowI[0:TP, :], src[0:N].rearrange("(t p) -> p t", p=TP)).then_inc(ld_w, 16)
            sp.wait_ge(diag_zero, 2)
            for c0, a in ((0, a_dst), (H, a_src)):
                for h in range(H):
                    p0 = h * (D // H) % P
                    sp.dma_start(a1[p0:p0 + D // H, h * (D // H) // P, c0 + h:c0 + h + 1],
                                 a[h, :].rearrange("(d a) -> d a", a=1)).then_inc(diag_ready, 16)
            for c0, a in ((0, attn_r), (H2, attn_l)):
                for h in range(H2):
                    p0 = h * (D // H2) % P
                    sp.dma_start(a2[p0:p0 + D // H2, h * (D // H2) // P, c0 + h:c0 + h + 1],
                                 a[h, :].rearrange("(d a) -> d a", a=1)).then_inc(diag_ready, 16)
            sp.wait_ge(rec_built, 3)
            sp.dma_start(rec_tab[0:E, :].rearrange("(p e) r -> p e r", e=EW), recF).then_inc(rec_stored, 16)
            sp.dma_start(rec_tab[E:E + P, :], padrec).then_inc(rec_stored, 16)
            sp.wait_ge(steps_ready, 2)
            sp.dma_start(step_tab.rearrange("w (g p) -> p w g", p=P), tabI[:, :, :]).then_inc(steps_stored, 16)
            sp.wait_ge(steps_stored, 16)
            sp.dma_start(rows[0:1, :, :], step_tab.rearrange("(a w) s -> a w s", a=1)).then_inc(steps_back, 16)
            sp.dma_start(blkb[:, :], step_tab[0, 0:STEPS].partition_broadcast(P)).then_inc(steps_back, 16)
            sp.wait_ge(steps_back, 32)
            sp.wait_ge(rec_stored, 32)
            with sp.Fori(0, ROUNDS) as i:
                first_edges = nc.values_load_multi_w_load_instructions(
                    rows[0:1, 1, bass.ds(i * U, U)], engines=[mybir.EngineType.SP], min_val=0, max_val=E,
                    skip_runtime_bounds_check_because=NOTE_E)[1]
                for k in range(U):
                    sp.dma_start(recs[:, bass.ds(i * U + k, 1), :].rearrange("p a r -> p (a r)"),
                                 rec_tab[bass.ds(first_edges[k], P), :]).then_inc(recs_in, 16)

            def store_tiles(e, jobs, waits):
                for i in range(TR):
                    for s in waits:
                        sp.wait_ge(s, C + e * NT + (i + 1) * UT)
                    for tab, st in jobs:
                        sp.dma_start(tab[i * UT * TP:(i + 1) * UT * TP, :].rearrange("(t p) c -> p t c", p=TP),
                                     st[0:TP, i * UT:(i + 1) * UT, :]).then_inc(tab_stored, 16)
            store_tiles(0, ((k_tab, KST), (v_tab, VST)), (ev_act, ev_dve))
            store_tiles(1, ((hw_tab, QT[:, :, 0:D]), (ss_tab, SL8[:, :, :])), (ev_act,))
            store_tiles(2, ((xt_tab, QT), (sl_tab, QT[:, :, D + H2:W1])), (ev_act,))
            sp.wait_ge(acc_done, C + 2 * STEPS)
            for q in range(4):
                sp.dma_start(BASES[:, 2 * q:2 * q + 2, :, :].rearrange("p b c o -> p (b c) o"),
                             bases[2 * q:2 * q + 2].rearrange("b (c p) o -> p (b c) o", p=P)).then_inc(xst_free[q], 16)
            with sp.Fori(0, NT) as t:
                for q in range(4):
                    sp.wait_ge(xw_copied_a, t * 8 + 2 * q + 2 + C)
                    sp.wait_ge(xw_copied_v, t * 8 + 2 * q + 2 + C)
                    sp.dma_start(xw_tab.rearrange("(n r) o -> n (r o)", r=R)[bass.ds(t * TP, TP), q * XC:(q + 1) * XC],
                                 xst[q][0:TP, :]).then_inc(xst_free[q], 16)
            sp.wait_ge(x_final, 1)
            sp.dma_start(out.rearrange("(t p) d -> p t d", p=TP), X[0:TP]).then_inc(out_stored, 16)
            sp.wait_ge(out_stored, 16)

        @block.gpsimd
        def _(pool):
            n = [0]

            def link(ins):
                n[0] += 1
                ins.then_inc(pool_line, 1)
                pool.wait_ge(pool_line, n[0])
            link(nc.gpsimd.memset(ident[:, :], 0.0))
            nc.gpsimd.affine_select(out=ident[:, :], in_=ident[:, :], compare_op=ALU.not_equal, fill=1.0, base=0,
                                    pattern=[[-1, P]], channel_multiplier=1).then_inc(const_ready, 1)
            nc.gpsimd.memset(ones[:, :], 1.0).then_inc(const_ready, 1)
            nc.gpsimd.memset(a1[:, :, :], 0.0).then_inc(diag_zero, 1)
            nc.gpsimd.memset(a2[:, :, :], 0.0).then_inc(diag_zero, 1)
            nc.gpsimd.iota(nodeI[:, :], pattern=[[1, TP]], base=0, channel_multiplier=0).then_inc(const_ready, 1)
            nc.gpsimd.iota(gridI[:, :], pattern=[[P, GRP]], base=0, channel_multiplier=1).then_inc(const_ready, 1)
            link(nc.gpsimd.memset(padrec[:, :], 0.0))
            nc.gpsimd.memset(padrec[:, 0:1], FAR).then_inc(rec_built, 1)

            def gathers(p, table, width, index, used, used_base):
                def half(i, h):
                    pool.wait_ge(used, i * U + (used_base + C + h * HALF - HALF))
                    nc.gpsimd.tensor_copy(stage[:, h, :], index[:, bass.ds(i * U + h * HALF, HALF)]).then_inc(staged, 1)
                    pool.wait_ge(staged, i * 2 + (2 * p * ROUNDS + h + 1))
                    pool.nop(nofuse=True)
                    for k in range(h * HALF, (h + 1) * HALF):
                        pool.indirect_dma_start(
                            ring[:, k, 0:width], None, table,
                            bass.IndirectOffsetOnAxis(ap=stage[:, h, k - h * HALF:k - h * HALF + 1], axis=0)
                        ).then_inc(got[k], 16)
                with pool.Fori(0, ROUNDS) as i:
                    half(i, 0)
                    half(i, 1)
            pool.wait_ge(idx_ready, 3)
            pool.wait_ge(tab_stored, 16 * 2 * TR)
            gathers(A0, k_tab, D, idx, prod_ready, 0)
            pool.wait_ge(prod_ready, C + STEPS)
            gathers(B0, v_tab, D, idx, msg_ready, 0)
            pool.wait_ge(tab_stored, 16 * 4 * TR)
            gathers(A1, ss_tab, H, idx, ss_copied, 0)
            pool.wait_ge(ss_copied, C + STEPS)
            gathers(B1, hw_tab, D, idx, msg_ready, STEPS)
            pool.wait_ge(tab_stored, 16 * 6 * TR)
            pool.wait_ge(ld_w, 16 * 14)
            for t in range(NT):
                pool.indirect_dma_start(ACC[0:TP, t, :], None, xt_tab,
                                        bass.IndirectOffsetOnAxis(ap=colI[0:TP, t:t + 1], axis=0)).then_inc(edge_rows, 16)
                pool.indirect_dma_start(SL[0:TP, t, :], None, sl_tab,
                                        bass.IndirectOffsetOnAxis(ap=rowI[0:TP, t:t + 1], axis=0)).then_inc(edge_rows, 16)
            for q in range(4):
                pool.wait_ge(xst_free[q], 16 * (NT + 1))
            gathers(B3, xw_tab, D, idx3, agg_ready, 2 * STEPS)

        @block.scalar
        def _(act):
            for s in ACT_PACED:
                act.sem_inc(s, C)
            act.wait_ge(ld_edge, 80)
            nc.scalar.activation(recF[:, :, 3:4], wF.rearrange("p (e a) -> p e a", a=1), ACT.Copy).then_inc(act_line, 1)
            nc.scalar.activation(recF[:, :, 4:7], atF, ACT.Copy).then_inc(rec_built, 1)

            def layer_std(layer):
                act.wait_ge(var_ready, layer + 1)
                nc.scalar.activation(std[0:TP, :], std[0:TP, :], ACT.Sqrt).then_inc(std_ready, 1)

            def hidden(q, layer, evac=None, unroll=UT):
                act.wait_ge(ln_ready, layer + 1)
                with act.Fori(0, TR) as i:
                    for k in range(UT):
                        t = i * UT + k
                        act.wait_ge(hT_ps, t + (q * NT + C - UT + 1))
                        nc.scalar.activation(Hb[0:TP, k, :], X[0:TP, bass.ds(t, 1), :].rearrange("p a d -> p (a d)"),
                                             ACT.Relu, bias=nmr[0:TP, bass.ds(t, 1)],
                                             scale=rstd[0:TP, bass.ds(t, 1)]).then_inc(h_ready, 1)
                        if evac and k >= 1:
                            evac(i * UT + (k - 1), k - 1)
                    if evac:
                        evac(i * UT + (UT - 1), UT - 1)

            def copy_ohT(a, s, k, n):
                act.wait_ge(ohT_ps, s + (a * STEPS + C + 1))
                act.wait_ge(qd_ready, s + (a * STEPS + C - 1))
                nc.scalar.activation(ohT[0:n, k % 2, :], tr[k % 2][0:n, 0:P], ACT.Copy).then_inc(ohT_copied, 1)

            layer_std(0)

            def evac_qkv(t, k):
                act.wait_ge(mm_done, t + (QKV * NT + C + 1))
                nc.scalar.activation(QT[0:TP, bass.ds(t, 1), 0:D].rearrange("p a d -> p (a d)"),
                                     mm[2 * (k % 2)][0:TP, 0:D], ACT.Copy,
                                     scale=float(D // H) ** -0.5).then_inc(act_line, 1)
                nc.scalar.activation(KST[0:TP, bass.ds(t, 1), :].rearrange("p a d -> p (a d)"),
                                     mm[2 * (k % 2)][0:TP, D:2 * D], ACT.Copy).then_inc(ev_act, 1)
            act.wait_ge(key_copied, NB)
            act.wait_ge(recs_in, 16 * STEPS)
            hidden(QKV, 0, evac_qkv)

            def pass_a0(i, last):
                for k in range(U):
                    copy_ohT(0, i * U + k, k, TP)
            rounds(act, pass_a0)

            def softmax_rows(a):
                for b in range(NB):
                    j0, j1 = 4 * b, 4 * b + 4
                    act.wait_ge(row_ps, C + a * NB + b + 1)
                    nc.scalar.activation(RS[:, j0 * P:j1 * P], bank[b][0:RW, :],
                                         ACT.Copy).then_inc(row_exp, 1)
                act.wait_ge(rows_shifted, a + 1)
                nc.scalar.activation(RF, RF, ACT.Exp).then_inc(row_exp, 1)
                for b in range(NB):
                    j0, j1 = 4 * b, 4 * b + 4
                    act.wait_ge(col_ps, C + a * NB + b + 1)
                    nc.scalar.activation(
                        SC[:, j0 * CH:j1 * CH, :].rearrange("p (j c) h -> p j (c h)", c=CH),
                        bank[b][:, :].rearrange("p (j r) -> p j r", r=P)[:, :, 0:RW],
                        ACT.Copy).then_inc(ex_ready, 1)
            softmax_rows(0)

            act.wait_ge(msg_ready, C + STEPS)
            with act.Fori(0, TR) as i:
                for k in range(UT):
                    t = i * UT + k
                    act.wait_ge(pre_d, t + (C - UT + 1))
                    nc.scalar.activation(resid[0:TP, k, :], X[0:TP, bass.ds(t, 1), :].rearrange("p a d -> p (a d)"),
                                         ACT.Relu, bias=nmr[0:TP, bass.ds(t, 1)],
                                         scale=rstd[0:TP, bass.ds(t, 1)]).then_inc(pre_h, 1)
            layer_std(1)

            def evac_lin1(t, k):
                act.wait_ge(mm_done, t + (LIN1 * NT + C + 1))
                nc.scalar.activation(QT[0:TP, bass.ds(t, 1), :].rearrange("p a d -> p (a d)"),
                                     mm[2 * (k % 2)][0:TP, 0:W1], ACT.Copy).then_inc(act_line, 1)
                nc.scalar.activation(SL8[0:TP, bass.ds(t, 1), :].rearrange("p a d -> p (a d)"),
                                     mm[2 * (k % 2)][0:TP, W1:W1 + H], ACT.Copy).then_inc(ev_act, 1)
            hidden(LIN1, 1, evac_lin1)

            def pass_a1(i, last):
                for k in range(U):
                    s = i * U + k
                    if k % HALF == 0:
                        act.wait_ge(ohT_ps, s + (STEPS + C))
                        nc.scalar.activation(oh[:, 0:HALF, TP:P], recs[:, bass.ds(s, HALF), 4:7],
                                             ACT.Copy).then_inc(attr_in, 1)
                    copy_ohT(1, s, k, P)
                    act.wait_ge(enc_ps, s + (C + 1))
                    act.wait_ge(prod_ready, s + (STEPS + C - 1))
                    nc.scalar.activation(enc[:, k % 2, :], mm[2 + k % 2][:, 0:D], ACT.Relu).then_inc(enc_copied, 1)
                    act.wait_ge(got[k], i * 16 + (A1 * ROUNDS * 16 + 16))
                    nc.scalar.activation(SS[:, bass.ds(place(i, k), 1), :].rearrange("p a h -> p (a h)"), ring[:, k, 0:H],
                                         ACT.Copy).then_inc(ss_copied, 1)
            rounds(act, pass_a1)
            softmax_rows(1)
            layer_std(2)

            def evac_lin2(t, k):
                act.wait_ge(mm_done, t + (LIN2 * NT + C + 1))
                nc.scalar.activation(QT[0:TP, bass.ds(t, 1), :].rearrange("p a d -> p (a d)"),
                                     mm[2 * (k % 2)][0:TP, 0:W1], ACT.Copy).then_inc(ev_act, 1)
            hidden(LIN2, 2, evac_lin2)
            act.wait_ge(sc_final, 3)
            nc.scalar.activation(s2[0:TP], s2[0:TP], ACT.Exp).then_inc(row_exp, 1)
            layer_std(3)

            def evac_xw(i, k):
                for j in range(8):
                    c = 2 * j
                    act.wait_ge(xw_ps, (i * UT + k) * 16 + (c + 1 + C))
                    act.wait_ge(xst_free[j // 2], (i * UT + k) * 16 + 16)
                    nc.scalar.activation(xst[j // 2][0:TP, (c % 4) * 512:(c % 4 + 1) * 512], mm[c % 4][0:TP, :],
                                         ACT.Copy).then_inc(xw_copied_a, 1)
            act.wait_ge(ln_ready, 4)
            with act.Fori(0, TR) as i:
                for k in range(UT):
                    t = i * UT + k
                    act.wait_ge(hT_ps, t + (XW * NT + C - UT + 1))
                    nc.scalar.activation(Hb[0:TP, k, :], X[0:TP, bass.ds(t, 1), :].rearrange("p a d -> p (a d)"),
                                         ACT.Relu, bias=nmr[0:TP, bass.ds(t, 1)],
                                         scale=rstd[0:TP, bass.ds(t, 1)]).then_inc(h_ready, 1)
                    if k >= 1:
                        evac_xw(i, k - 1)
                evac_xw(i, UT - 1)

        @block.tensor
        def _(pe):
            for s in PE_PACED:
                pe.sem_inc(s, C)
            pe.wait_ge(const_ready, 4)
            pe.wait_ge(cnt_ready, 1)
            nc.tensor.matmul(mm[0][:, 0:NT], ones[0:TP, :], cnt[0:TP, :], start=True, stop=True).then_inc(first_ps, 1)
            pe.wait_ge(ld_w, 16 * 14)
            pe.wait_ge(diag_ready, 16 * (2 * H + 2 * H2))
            for w, (wn, a) in enumerate(((w1n, a1), (w2n, a2))):
                for c in range(KC):
                    for o in range(KC):
                        last = nc.tensor.matmul(ag[w][:, c * 16:c * 16 + a.shape[2]], wn[:, o, c * P:(c + 1) * P],
                                                a[:, o, :], start=(o == 0), stop=(o == KC - 1))
                last.then_inc(wa_ps, 1)
            pe.wait_ge(idx_ready, 3)
            for b in range(NB):
                if b >= 4:
                    pe.wait_ge(key_copied, b - 3)
                for j in range(4 * b, 4 * b + 4):
                    last = nc.tensor.transpose(mm[b % 4][0:RW, (j % 4) * P:(j % 4 + 1) * P],
                                               SC[:, j * CH:(j + 1) * CH, :].rearrange("p c h -> p (c h)"), ident[:, :])
                last.then_inc(key_ps, 1)

            def column_to_row(n, first_col, last_col):
                pe.wait_ge(edge_ready, n)
                for c in range(first_col, last_col):
                    last = nc.tensor.transpose(tr[0][0:1, c * P:c * P + RW], edge[:, c:c + 1], ident[0:RW, 0:RW])
                last.then_inc(edge_ps, 1)

            def row_to_column(n, row):
                pe.wait_ge(line_ready, n)
                nc.tensor.matmul(tr[1][0:RW, 0:1], line_[0:1, row, :], ones[0:1, 0:1], start=True,
                                 stop=True).then_inc(init_ps, 1)
            column_to_row(1, 0, 3)

            def tiles(q, product, src=None, ready=None, ready_base=0):
                def turn(i, k):
                    t = i * UT + k
                    if ready is None:
                        pe.wait_ge(h_ready, t + ((q - (q > POST0)) * NT + C + 1))
                    else:
                        pe.wait_ge(ready, t + (ready_base + 1))
                    pe.wait_ge(hT_copied, t + (q * NT + C - (0 if k == 0 else 1)))
                    for c in range(KC):
                        last = nc.tensor.transpose(tr[k % 2][:, c * P:c * P + TP],
                                                   (Hb if src is None else src)[0:TP, k, c * P:(c + 1) * P],
                                                   ident[0:TP, 0:TP])
                    last.then_inc(hT_ps, 1)
                with pe.Fori(0, TR) as i:
                    turn(i, 0)
                    for k in range(UT):
                        if k + 1 < UT:
                            turn(i, k + 1)
                        pe.wait_ge(hT_copied, i * UT + (k + q * NT + C + 1))
                        product(i, k)

            def banks_free(e, i, k, sems):
                for s in sems:
                    pe.wait_ge(s, i * UT + (k + e * NT + C - (0 if k == 0 else 1)))

            def dense(bankap, k, w, lo, hi, bias=None):
                for c in range(KC):
                    last = nc.tensor.matmul(bankap, HT[:, k, c, 0:TP], w[:, c, lo:hi], start=(c == 0),
                                            stop=(c == KC - 1 and bias is None))
                if bias is not None:
                    last = nc.tensor.matmul(bankap, ones[0:1, 0:TP], bias[0:1, lo:hi], start=False, stop=True)
                return last

            def product_qkv(i, k):
                banks_free(0, i, k, (ev_act, ev_dve))
                dense(mm[2 * (k % 2)][0:TP, 0:2 * D], k, wqkv, 0, 2 * D, bqkv)
                dense(mm[2 * (k % 2) + 1][0:TP, 0:D], k, wqkv, 2 * D, 3 * D, bqkv).then_inc(mm_done, 1)
            pe.wait_ge(key_copied, NB)
            pe.wait_ge(line_in, 1)
            tiles(QKV, product_qkv)

            def transpose_oh(p, a, i, k, rows_):
                s = i * U + k
                pe.wait_ge(oh_ready, s + (p * STEPS + C + 1))
                pe.wait_ge(ohT_copied, s + (a * STEPS + C - 1))
                nc.tensor.transpose(tr[k % 2][0:rows_, 0:P], oh[:, k % OHB, 0:rows_], ident[:, :]).then_inc(ohT_ps, 1)

            def pass_a0(i, last):
                blk = round_blocks(mybir.EngineType.PE, i)
                for k in range(U):
                    s = i * U + k
                    if k == 0:
                        transpose_oh(A0, 0, i, 0, TP)
                    if k + 1 < U:
                        transpose_oh(A0, 0, i, k + 1, TP)
                    pe.wait_ge(ohT_copied, s + (C + 1))
                    pe.wait_ge(prod_ready, s + (C - 1))
                    nc.tensor.matmul(mm[k % 2][:, 0:D], ohT[0:TP, k % 2, :],
                                     QT[0:TP, bass.ds(blk[k], 1), 0:D].rearrange("p a d -> p (a d)"),
                                     start=True, stop=True).then_inc(qd_ready, 1)
            rounds(pe, pass_a0)

            def softmax_rows(a):
                pe.wait_ge(sc_final, a + 1)
                for b in range(NB):
                    for j in range(4 * b, 4 * b + 4):
                        last = nc.tensor.transpose(bank[b][0:RW, (j % 4) * P:(j % 4 + 1) * P],
                                                   SC[:, j * CH:(j + 1) * CH, :].rearrange("p c h -> p (c h)"), ident[:, :])
                    last.then_inc(row_ps, 1)
                pe.wait_ge(row_exp, a * (NB + 1) + NB)
                column_to_row(2 + 2 * a, 3, 4)
                row_to_column(2 * a + 1, 7)
                column_to_row(3 + 2 * a, 3, 4)
                row_to_column(2 * a + 2, 8)
                pe.wait_ge(row_exp, (a + 1) * (NB + 1))
                for b in range(NB):
                    for j in range(4 * b, 4 * b + 4):
                        last = nc.tensor.transpose(bank[b][:, (j % 4) * P:(j % 4) * P + RW],
                                                   RF[:, j * P:(j + 1) * P], ident[0:RW, 0:RW])
                    last.then_inc(col_ps, 1)
            softmax_rows(0)

            def pass_b(p, b, weighted):
                def body(i, last):
                    for k in range(U):
                        s = i * U + k
                        pe.wait_ge(oh_ready, s + (p * STEPS + C + 1))
                        pe.wait_ge(acc_done, s + (b * STEPS + C - 1))
                        if weighted:
                            pe.wait_ge(msg_ready, s + (b * STEPS + C + 1))
                            nc.tensor.matmul(ag[k % 2][0:TP, 0:D], oh[:, k % OHB, 0:TP], msg[:, k % MB, :],
                                             start=True, stop=True)
                            nc.tensor.matmul(ag[k % 2][0:TP, D:W1], oh[:, k % OHB, 0:TP],
                                             SC[:, bass.ds(place(i, k), 1), :].rearrange("p a h -> p (a h)"),
                                             start=True, stop=True).then_inc(agg_ready, 1)
                        else:
                            pe.wait_ge(got[k], i * 16 + (p * ROUNDS * 16 + 16))
                            nc.tensor.matmul(ag[k % 2][0:TP, 0:D], oh[:, k % OHB, 0:TP], ring[:, k, :],
                                             start=True, stop=True).then_inc(agg_ready, 1)
                rounds(pe, body)
            pe.wait_ge(ex_ready, NB)
            pass_b(B0, 0, True)

            def product_post0(i, k):
                pe.wait_ge(x_done, i * UT + (k + C - (0 if k == 0 else 1)))
                dense(mm[2 * (k % 2)][0:TP, 0:D], k, wout, 0, D, bout).then_inc(mm_done, 1)
            tiles(POST0, product_post0, Hb, pre_d, C)

            def product_lin1(i, k):
                banks_free(1, i, k, (ev_act,))
                dense(mm[2 * (k % 2)][0:TP, 0:D + 2 * H], k, w1c, 0, D + 2 * H).then_inc(mm_done, 1)
            pe.wait_ge(wa_ready, 2)
            tiles(LIN1, product_lin1)

            def pass_a1(i, last):
                blk = round_blocks(mybir.EngineType.PE, i)
                for k in range(U):
                    s = i * U + k
                    if k % HALF == 0:
                        pe.wait_ge(attr_in, i * 2 + (k // HALF + C + 1))
                        transpose_oh(A1, 1, i, k, P)
                    if (k + 1) % HALF:
                        transpose_oh(A1, 1, i, k + 1, P)
                    pe.wait_ge(ohT_copied, s + (STEPS + C + 1))
                    pe.wait_ge(enc_copied, s + (C - 1))
                    nc.tensor.matmul(mm[2 + k % 2][:, 0:D], ohT[:, k % 2, :], encw[:, :],
                                     start=True, stop=True).then_inc(enc_ps, 1)
                    pe.wait_ge(sdst_added, s + (C - 1))
                    nc.tensor.matmul(mm[k % 2][:, 0:W1], ohT[0:TP, k % 2, :],
                                     QT[0:TP, bass.ds(blk[k], 1), :].rearrange("p a d -> p (a d)"),
                                     start=True, stop=True).then_inc(qd_ready, 1)
            rounds(pe, pass_a1)
            softmax_rows(1)
            pe.wait_ge(ex_ready, 2 * NB)
            pass_b(B1, 1, True)

            def product_lin2(i, k):
                banks_free(2, i, k, (ev_act,))
                dense(mm[2 * (k % 2)][0:TP, 0:W1], k, w2c, 0, W1).then_inc(mm_done, 1)
            tiles(LIN2, product_lin2)

            def product_xw(i, k):
                wr = WR.rearrange("p c r o -> p c (r o)")
                for c in range(R * D // 512):
                    pe.wait_ge(xw_copied_v if c % 2 else xw_copied_a, (i * UT + k) * 8 + (c // 2 + C - 1))
                    dense(mm[c % 4][0:TP, :], k, wr, c * 512, (c + 1) * 512).then_inc(xw_ps, 1)
            pe.wait_ge(wr_ready, 1)
            tiles(XW, product_xw)
            pass_b(B3, 2, False)

        @block.vector
        def _(dve):
            for s in DVE_PACED:
                dve.sem_inc(s, C)
            n = [0]

            def link(ins):
                n[0] += 1
                ins.then_inc(dve_line, 1)
                dve.wait_ge(dve_line, n[0])
            V = nc.vector
            dve.wait_ge(const_ready, 4)
            dve.wait_ge(ld_edge, 80)
            V.tensor_copy(node[:, :], nodeI[:, :]).then_inc(dve_line, 1)
            V.tensor_copy(grid[:, :], gridI[:, :]).then_inc(dve_line, 1)
            V.tensor_copy(recF[:, :, 0], dstI).then_inc(dve_line, 1)
            V.tensor_copy(recF[:, :, 1], srcI).then_inc(dve_line, 1)
            V.tensor_copy(recF[:, :, 2], typI).then_inc(dve_line, 1)
            V.memset(cnt[:, :], float(EW)).then_inc(dve_line, 1)
            n[0] += 6
            dve.wait_ge(dve_line, n[0])
            V.scalar_tensor_tensor(out=recF[:, :, 7], in0=recF[:, :, 1], scalar=float(R), in1=recF[:, :, 2],
                                   op0=ALU.mult, op1=ALU.add).then_inc(rec_built, 1)
            for b in range(1, NT):
                V.tensor_scalar(junk, recF[:, :, 0], float(TP * b), 0.0, ALU.is_lt, ALU.add,
                                accum_out=cnt[0:EP, b - 1:b]).then_inc(dve_line, 1)
                n[0] += 1
                dve.wait_ge(dve_line, n[0])
            V.memset(first[:, :], 0.0).then_inc(cnt_ready, 1)
            dve.wait_ge(cnt_ready, 1)
            dve.wait_ge(first_ps, 1)
            link(V.tensor_copy(first[:, 1:NT + 1], mm[0][:, 0:NT]))
            link(V.tensor_tensor(ne[:, :], first[:, 1:NT + 1], first[:, 0:NT], ALU.subtract))
            link(V.tensor_scalar(nsI[:, :], ne[:, :], float(P - 1), None, ALU.add))
            link(V.tensor_scalar(nsI[:, :], nsI[:, :], P.bit_length() - 1, None, ALU.logical_shift_right))
            link(V.tensor_copy(ns[:, :], nsI[:, :]))
            link(V.tensor_tensor_scan(cum[:, :], ones[:, 0:NT], ns[:, :], 0.0, ALU.mult, ALU.add))
            link(V.scalar_tensor_tensor(out=gap[:, :], in0=ns[:, :], scalar=-float(P), in1=ne[:, :],
                                        op0=ALU.mult, op1=ALU.add))
            for g in range(GRP):
                link(V.tensor_scalar(mask[:, 0:NT - 1], cum[:, 0:NT - 1], grid[:, g:g + 1], 0.0, ALU.is_le, ALU.add,
                                     accum_out=blkF[:, g:g + 1]))
                link(V.tensor_tensor(mask[:, 0:NT - 1], mask[:, 0:NT - 1], gap[:, 0:NT - 1], ALU.mult))
                link(V.tensor_reduce(estF[:, g:g + 1], mask[:, 0:NT - 1], AX.X, ALU.add))
            link(V.scalar_tensor_tensor(out=estF[:, :], in0=grid[:, :], scalar=float(P), in1=estF[:, :],
                                        op0=ALU.mult, op1=ALU.add))
            link(V.tensor_scalar(estF[:, :], estF[:, :], float(E), None, ALU.min))
            V.tensor_copy(tabI[:, 0, :], blkF[:, :]).then_inc(steps_ready, 1)
            V.tensor_copy(tabI[:, 1, :], estF[:, :]).then_inc(steps_ready, 1)
            dve.wait_ge(wa_ps, 1)
            V.tensor_copy(w1c[:, :, D:D + 2 * H], ag[0][:, 0:32].rearrange("p (c a) -> p c a", a=16)).then_inc(wa_ready, 1)
            dve.wait_ge(wa_ps, 2)
            V.tensor_copy(w2c[:, :, D:D + 2 * H2],
                          ag[1][:, 0:32].rearrange("p (c a) -> p c a", a=16)[:, :, 0:2 * H2]).then_inc(wa_ready, 1)

            def layernorm(layer):
                if layer == 0:
                    dve.wait_ge(ld_x, 16)
                with dve.Fori(0, TR) as i:
                    for k in range(UT):
                        t = i * UT + k
                        V.bn_stats(st6[0:TP, bass.ds(t, 1), :].rearrange("p a c -> p (a c)"),
                                   X[0:TP, bass.ds(t, 1), :].rearrange("p a d -> p (a d)")).then_inc(bn_s, 1)
                dve.wait_ge(bn_s, (layer + 1) * NT + C)
                me, mo, q = (lnw[0:TP, j, :] for j in range(3))
                link(V.tensor_tensor(me, st6[0:TP, :, 1], st6[0:TP, :, 4], ALU.add))
                link(V.tensor_tensor(mo, st6[0:TP, :, 1], st6[0:TP, :, 4], ALU.subtract))
                link(V.tensor_tensor(q, st6[0:TP, :, 2], st6[0:TP, :, 5], ALU.add))
                link(V.scalar_tensor_tensor(out=mo, in0=mo, scalar=0.25, in1=mo, op0=ALU.mult, op1=ALU.mult))
                link(V.scalar_tensor_tensor(out=q, in0=q, scalar=1.0 / D, in1=mo, op0=ALU.mult, op1=ALU.add))
                V.tensor_scalar(std[0:TP, :], q, EPS, None, ALU.add).then_inc(var_ready, 1)
                dve.wait_ge(std_ready, layer + 1)
                link(V.reciprocal(rstd[0:TP, :], std[0:TP, :]))
                V.scalar_tensor_tensor(out=nmr[0:TP, :], in0=me, scalar=-0.5, in1=rstd[0:TP, :],
                                       op0=ALU.mult, op1=ALU.mult).then_inc(ln_ready, 1)
            layernorm(0)

            dve.wait_ge(steps_back, 32)
            dve.wait_ge(recs_in, 16 * STEPS)
            link(V.scalar_tensor_tensor(out=dloc[:, :], in0=blkb[:, :], scalar=-float(TP), in1=recs[:, :, 0],
                                        op0=ALU.mult, op1=ALU.add))
            link(V.tensor_scalar(key[:, :], dloc[:, :], float(TP), FAR, ALU.is_ge, ALU.mult))
            link(V.tensor_tensor(key[:, :], key[:, :], recs[:, :, 0], ALU.add))
            V.tensor_copy(SC.rearrange("p (j c) h -> p j c h", c=CH),
                          key[:, :].rearrange("p (c j) -> p j c", j=JS).unsqueeze(3).broadcast_to([P, JS, CH, H])
                          ).then_inc(idx_ready, 1)
            V.tensor_copy(idx[:, :], recs[:, :, 1]).then_inc(idx_ready, 1)
            V.tensor_copy(idx3[:, :], recs[:, :, 7]).then_inc(idx_ready, 1)
            for b in range(NB):
                j0, j1 = 4 * b, 4 * b + 4
                dve.wait_ge(key_ps, C + b + 1)
                V.tensor_copy(KR[:, j0 * P:j1 * P], mm[b % 4][0:RW, :]).then_inc(key_copied, 1)
            dve.wait_ge(key_copied, NB)
            link(V.memset(PEN[:, :], 0.0))
            link(V.tensor_tensor(RF[:, 0:RL - 1], KR[:, 1:RL], KR[:, 0:RL - 1], ALU.not_equal))
            link(V.tensor_scalar(PEN[:, 1:RL], RF[:, 0:RL - 1], NEG, None, ALU.mult))
            link(V.tensor_copy(edge[:, 0:1], KR[:, 0:1]))
            link(V.tensor_copy(edge[:, 1:2], KR[:, RL - 1:RL]))
            V.tensor_reduce(edge[:, 2:3], PEN[:, 0:RL], AX.X, ALU.min).then_inc(edge_ready, 1)
            dve.wait_ge(edge_ps, 1)
            V.tensor_copy(line_[0:1, 0:3, :], tr[0][0:1, 0:3 * P].rearrange("p (a b) -> p a b", b=P)[:, :, 0:RW]
                          ).then_inc(line_in, 1)
            dve.wait_ge(line_in, 1)
            link(V.memset(line_[0:1, 3:10, :], NEG))
            link(V.tensor_tensor(line_[0:1, 3, H:RW], line_[0:1, 0, H:RW], line_[0:1, 1, 0:RW - H], ALU.not_equal))
            link(V.tensor_scalar(line_[0:1, 3, H:RW], line_[0:1, 3, H:RW], NEG, None, ALU.mult))
            link(V.tensor_tensor(line_[0:1, 4, :], line_[0:1, 3, :], line_[0:1, 2, :], ALU.add))
            link(V.tensor_tensor(line_[0:1, 5, 0:RW - H], line_[0:1, 3, H:RW], line_[0:1, 2, 0:RW - H], ALU.add))

            def hT_copies(q, extra=None):
                with dve.Fori(0, TR) as i:
                    for k in range(UT):
                        if extra:
                            extra(i, k, 0)
                        t = i * UT + k
                        dve.wait_ge(hT_ps, t + (q * NT + C + 1))
                        if q == XW:
                            dve.wait_ge(xw_ps, t * 16 + (C - UT * 16 + 16))
                        else:
                            dve.wait_ge(mm_done, t + (q * NT + C - UT + 1))
                        V.tensor_copy(HT[:, k, :, 0:TP],
                                      tr[k % 2][:, 0:2 * P].rearrange("p (c n) -> p c n", c=KC)[:, :, 0:TP]
                                      ).then_inc(hT_copied, 1)
                        if extra and k >= 1:
                            extra(i, k - 1, 1)
                    if extra:
                        extra(i, UT - 1, 1)

            def evac_v(i, k, late):
                if late:
                    dve.wait_ge(mm_done, i * UT + (k + QKV * NT + C + 1))
                    V.tensor_copy(VST[0:TP, bass.ds(i * UT + k, 1), :].rearrange("p a d -> p (a d)"),
                                  mm[2 * (k % 2) + 1][0:TP, 0:D]).then_inc(ev_dve, 1)
            hT_copies(QKV, evac_v)

            def one_hot(p, i, k, free, free_base):
                s = i * U + k
                dve.wait_ge(free, s + (free_base + C - OHB + 1))
                if p == B3:
                    ins = V.tensor_scalar(oh[:, k % OHB, 0:TP], node[:, :], dloc[:, bass.ds(s, 1)],
                                          recs[:, bass.ds(s, 1), 3:4].rearrange("p a b -> p (a b)"),
                                          ALU.is_equal, ALU.mult)
                else:
                    ins = V.tensor_scalar(oh[:, k % OHB, 0:TP], node[:, :], dloc[:, bass.ds(s, 1)], None, ALU.is_equal)
                ins.then_inc(oh_ready, 1)
            AHEAD = 4

            def passes(p, free, free_base, step, blocks=False):
                for k in range(AHEAD):
                    one_hot(p, 0, k, free, free_base)

                def body(i, last):
                    blk = round_blocks(mybir.EngineType.DVE, i) if blocks else None
                    for k in range(U):
                        if not (last and k + AHEAD >= U):
                            one_hot(p, i if k + AHEAD < U else i + 1, (k + AHEAD) % U, free, free_base)
                        step(i, k, blk)
                rounds(dve, body)

            def score(i, k, a):
                s = i * U + k
                dve.wait_ge(prod_ready, s + (a * STEPS + C + 1))
                V.tensor_reduce(SC[:, bass.ds(place(i, k), 1), :].rearrange("p a h -> p (a h)"),
                                prod[:, k % 2, :].rearrange("p (h d) -> p h d", h=H), AX.X, ALU.add
                                ).then_inc(score_ready, 1)

            def step_a0(i, k, blk):
                s = i * U + k
                dve.wait_ge(qd_ready, s + (C + 1))
                dve.wait_ge(got[k], i * 16 + 16)
                dve.wait_ge(score_ready, s + (C - 1))
                V.tensor_tensor(prod[:, k % 2, :], mm[k % 2][:, 0:D], ring[:, k, :], ALU.mult).then_inc(prod_ready, 1)
                score(i, k, 0)
            dve.wait_ge(tab_stored, 16 * 2 * TR)
            passes(A0, ohT_ps, 0, step_a0)
            dve.wait_ge(score_ready, C + STEPS)
            dve.sem_inc(sc_final, 1)

            def softmax_rows(a):
                dve.wait_ge(row_exp, a * (NB + 1) + NB)
                link(V.tensor_tensor_scan(RF, PEN[:, 0:RL], RS, NEG, ALU.add, ALU.max))
                V.tensor_copy(edge[:, 3:4], RF[:, RL - 1:RL]).then_inc(edge_ready, 1)
                dve.wait_ge(edge_ps, 2 + 2 * a)
                link(V.tensor_copy(line_[0:1, 6, :], tr[0][0:1, 3 * P:3 * P + RW]))
                last = None
                for h in range(H):
                    last = V.tensor_tensor_scan(line_[0:1, 9, h:RW:H], line_[0:1, 4, h:RW:H], line_[0:1, 6, h:RW:H], NEG,
                                                ALU.add, ALU.max)
                link(last)
                V.tensor_tensor(line_[0:1, 7, H:RW], line_[0:1, 9, 0:RW - H], line_[0:1, 3, H:RW], ALU.add).then_inc(line_ready, 1)
                dve.wait_ge(init_ps, 2 * a + 1)
                link(V.tensor_copy(init[:, 0:1], tr[1][0:RW, 0:1]))
                link(V.tensor_tensor_scan(RF, PEN[:, 0:RL], RS, init[:, 0:1], ALU.add, ALU.max))
                back = PEN[:, 1:RL + 1][:, ::-1]
                link(V.tensor_tensor_scan(RM[:, ::-1], back, RF[:, ::-1], NEG, ALU.add, ALU.max))
                V.tensor_copy(edge[:, 3:4], RM[:, 0:1]).then_inc(edge_ready, 1)
                dve.wait_ge(edge_ps, 3 + 2 * a)
                link(V.tensor_copy(line_[0:1, 6, :], tr[0][0:1, 3 * P:3 * P + RW]))
                for h in range(H):
                    last = V.tensor_tensor_scan(line_[0:1, 9, h:RW:H][:, ::-1], line_[0:1, 5, h:RW:H][:, ::-1],
                                                line_[0:1, 6, h:RW:H][:, ::-1], NEG, ALU.add, ALU.max)
                link(last)
                V.tensor_tensor(line_[0:1, 8, 0:RW - H], line_[0:1, 9, H:RW], line_[0:1, 3, H:RW], ALU.add).then_inc(line_ready, 1)
                dve.wait_ge(init_ps, 2 * a + 2)
                link(V.tensor_copy(init[:, 1:2], tr[1][0:RW, 0:1]))
                link(V.tensor_tensor_scan(RM[:, ::-1], back, RF[:, ::-1], init[:, 1:2], ALU.add, ALU.max))
                V.tensor_tensor(RF, RS, RM, ALU.subtract).then_inc(rows_shifted, 1)
                dve.wait_ge(ex_ready, NB * (a + 1))
            softmax_rows(0)

            def step_b(p, b):
                def step(i, k, blk):
                    s = i * U + k
                    if b < 2:
                        dve.wait_ge(got[k], i * 16 + (p * ROUNDS * 16 + 16))
                        dve.wait_ge(agg_ready, s + (b * STEPS + C - MB + 1))
                        V.tensor_tensor(msg[:, k % MB, :].rearrange("p (h d) -> p h d", h=H),
                                        ring[:, k, :].rearrange("p (h d) -> p h d", h=H),
                                        SC[:, bass.ds(place(i, k), 1), :].rearrange("p a h -> p h a").broadcast_to([P, H, D // H]),
                                        ALU.mult).then_inc(msg_ready, 1)
                    if k >= 1:
                        accumulate(i, k - 1, blk, b)
                    if k == U - 1:
                        accumulate(i, k, blk, b)
                return step

            def accumulate(i, k, blk, b):
                s = i * U + k
                wide = W1 if b < 2 else D
                dve.wait_ge(agg_ready, s + (b * STEPS + C + 1))
                dve.wait_ge(acc_done, s + (b * STEPS + C))
                a = ACC[0:TP, bass.ds(blk[k], 1), 0:wide].rearrange("p a d -> p (a d)")
                V.tensor_tensor(a, a, ag[k % 2][0:TP, 0:wide], ALU.add).then_inc(acc_done, 1)
            link(V.memset(UNI[:, 0:QTN], 0.0))
            passes(B0, agg_ready, 0, step_b(B0, 0), True)
            dve.wait_ge(acc_done, C + STEPS)

            for_all = ACC[0:TP, :, D:W1]
            link(V.tensor_scalar(for_all, for_all, 1e-10, None, ALU.max))
            link(V.reciprocal(for_all, for_all))

            def heads(t):
                return ACC[0:TP, bass.ds(t, 1), 0:D].rearrange("p a (h d) -> p (a h) d", h=H)

            def inv_den(t):
                return ACC[0:TP, bass.ds(t, 1), D:W1].rearrange("p a h -> p h a").broadcast_to([TP, H, D // H])

            def post0(i, k, late):
                t = i * UT + k
                if not late:
                    dve.wait_ge(hT_ps, t + (POST0 * NT + C - UT + 1))
                    V.tensor_tensor(Hb[0:TP, k, :].rearrange("p (d h) -> p h d", h=H), heads(t), inv_den(t),
                                    ALU.mult).then_inc(pre_u, 1)
                    dve.wait_ge(pre_u, t + (C + 1))
                    dve.wait_ge(pre_h, t + 1)
                    V.tensor_tensor(Hb[0:TP, k, :], Hb[0:TP, k, :], resid[0:TP, k, :], ALU.add).then_inc(pre_d, 1)
                else:
                    dve.wait_ge(mm_done, t + (POST0 * NT + C + 1))
                    xt = X[0:TP, bass.ds(t, 1), :].rearrange("p a d -> p (a d)")
                    V.tensor_tensor(xt, xt, mm[2 * (k % 2)][0:TP, 0:D], ALU.add).then_inc(x_done, 1)
            hT_copies(POST0, post0)
            dve.wait_ge(x_done, C + NT)

            layernorm(1)
            hT_copies(LIN1)

            def step_a1(i, k, blk):
                s = i * U + k
                dve.wait_ge(enc_copied, s + (C + 1))
                dve.wait_ge(qd_ready, s + (STEPS + C + 1))
                dve.wait_ge(score_ready, s + (STEPS + C - 1))
                V.tensor_tensor(prod[:, k % 2, :], mm[k % 2][:, 0:D], enc[:, k % 2, :], ALU.mult).then_inc(prod_ready, 1)
                score(i, k, 1)
                sc = SC[:, bass.ds(place(i, k), 1), :].rearrange("p a h -> p (a h)")
                dve.wait_ge(score_ready, s + (STEPS + C + 1))
                V.tensor_tensor(sc, sc, mm[k % 2][:, D:W1], ALU.add).then_inc(sdst_added, 1)
            passes(A1, ohT_ps, STEPS, step_a1)
            dve.wait_ge(sdst_added, C + STEPS)
            dve.wait_ge(ss_copied, C + STEPS)
            link(V.tensor_tensor(SC, SC, SS, ALU.add))
            V.scalar_tensor_tensor(out=SC, in0=SC, scalar=0.2, in1=SC, op0=ALU.mult, op1=ALU.max).then_inc(sc_final, 1)
            softmax_rows(1)
            link(V.memset(UNI[:, 0:QTN], 0.0))
            passes(B1, agg_ready, STEPS, step_b(B1, 1), True)
            dve.wait_ge(acc_done, C + 2 * STEPS)
            link(V.tensor_scalar(for_all, for_all, 1e-10, None, ALU.max))
            link(V.reciprocal(for_all, for_all))
            link(V.tensor_tensor(ACC[0:TP, :, 0:D].rearrange("p t (h d) -> p t h d", h=H),
                                 ACC[0:TP, :, 0:D].rearrange("p t (h d) -> p t h d", h=H),
                                 for_all.unsqueeze(3).broadcast_to([TP, NT, H, D // H]), ALU.mult))
            link(V.tensor_tensor(X[0:TP], X[0:TP], ACC[0:TP, :, 0:D], ALU.add))
            link(V.tensor_tensor(X[0:TP], X[0:TP], bias1b[0:TP, :].unsqueeze(1).broadcast_to([TP, NT, D]), ALU.add))

            layernorm(2)
            hT_copies(LIN2)
            dve.wait_ge(edge_rows, 16 * 2 * NT)
            G = ACC[0:TP]
            a = s2[0:TP]
            link(V.tensor_tensor(a, SL[0:TP], G[:, :, D:D + H2], ALU.add))
            link(V.scalar_tensor_tensor(out=a, in0=a, scalar=0.01, in1=a, op0=ALU.mult, op1=ALU.max))
            link(V.tensor_reduce(m2[0:TP, 0, :], a, AX.X, ALU.max))
            V.tensor_tensor(a, a, m2[0:TP, 0, :].unsqueeze(2).broadcast_to([TP, NT, H2]), ALU.subtract).then_inc(sc_final, 1)
            dve.wait_ge(row_exp, 2 * NB + 3)
            link(V.tensor_reduce(m2[0:TP, 0, :], a, AX.X, ALU.add))
            link(V.reciprocal(m2[0:TP, 1, :], m2[0:TP, 0, :]))
            link(V.tensor_tensor(a, a, m2[0:TP, 1, :].unsqueeze(2).broadcast_to([TP, NT, H2]), ALU.mult))
            gh = G[:, :, 0:D].rearrange("p t (h d) -> p t h d", h=H2)
            link(V.tensor_tensor(gh, gh, a.unsqueeze(3).broadcast_to([TP, NT, H2, D // H2]), ALU.mult))
            link(V.tensor_reduce(o2[0:TP], G[:, :, 0:D].rearrange("p t (h d) -> p t d h", h=H2), AX.X, ALU.add))
            xh = X[0:TP].rearrange("p t (h d) -> p t h d", h=H2)
            link(V.tensor_tensor(xh, xh, o2[0:TP].unsqueeze(2).broadcast_to([TP, NT, H2, D // H2]), ALU.add))

            dve.wait_ge(ld_w, 16 * 14)
            for q in range(4):
                dve.wait_ge(xst_free[q], 16)
            for r in range(R):
                for b in range(B):
                    w = wcb[:, r * B + b:r * B + b + 1]
                    if b == 0:
                        link(V.tensor_scalar(WR[:, :, r, :], BASES[:, b, :, :], w, None, ALU.mult))
                    elif (r, b) != (R - 1, B - 1):
                        link(V.scalar_tensor_tensor(out=WR[:, :, r, :], in0=BASES[:, b, :, :], scalar=w,
                                                    in1=WR[:, :, r, :], op0=ALU.mult, op1=ALU.add))
                    else:
                        V.scalar_tensor_tensor(out=WR[:, :, r, :], in0=BASES[:, b, :, :], scalar=w,
                                               in1=WR[:, :, r, :], op0=ALU.mult, op1=ALU.add).then_inc(wr_ready, 1)
            layernorm(3)

            def evac_xw(i, k, late):
                if late:
                    for j in range(8):
                        c = 2 * j + 1
                        dve.wait_ge(xw_ps, (i * UT + k) * 16 + (c + 1 + C))
                        dve.wait_ge(xst_free[j // 2], (i * UT + k) * 16 + 16)
                        V.tensor_copy(xst[j // 2][0:TP, (c % 4) * 512:(c % 4 + 1) * 512],
                                      mm[c % 4][0:TP, :]).then_inc(xw_copied_v, 1)
            hT_copies(XW, evac_xw)
            for q in range(4):
                dve.wait_ge(xst_free[q], 16 * (NT + 1))
            link(V.memset(UNI[:, 0:QTN], 0.0))
            passes(B3, agg_ready, 2 * STEPS, step_b(B3, 2), True)
            dve.wait_ge(acc_done, C + 3 * STEPS)
            V.scalar_tensor_tensor(out=X[0:TP], in0=ACC[0:TP, :, 0:D], scalar=0.0, in1=X[0:TP],
                                   op0=ALU.max, op1=ALU.add).then_inc(x_final, 1)


IN = ("x", "src", "dst", "edge_attr_3", "edge_type_32", "edge_weight1", "L0_gnn_W_qkv", "L0_gnn_b_qkv",
      "L0_gnn_W_out", "L0_gnn_b_out", "L1_gnn_W", "L1_gnn_W:T", "L1_gnn_a_src", "L1_gnn_a_dst", "L1_gnn_edge_W:T",
      "L1_gnn_edge_b", "L1_gnn_bias", "L2_gnn_weight", "L2_gnn_weight:T", "L2_gnn_attn_l", "L2_gnn_attn_r",
      "L3_gnn_bases", "L3_gnn_w_comp")


def kernel(**inputs):
    import numpy as np
    import concourse.bacc as bacc
    from concourse.bass_utils import run_bass_kernel_spmd as run

    nc = bacc.Bacc("TRN2", target_bir_lowering=False, num_devices=1)
    arrays, args = {}, []
    for name in IN:
        a = np.asarray(inputs[name.split(":")[0]])
        if name.endswith(":T"):
            a = a.T
        a = np.ascontiguousarray(a)
        label = "in_" + name.replace(":", "_")
        arrays[label] = a
        args.append(nc.dram_tensor(label, a.shape, mybir.dt.from_np(a.dtype), kind="ExternalInput").ap())
    result = nc.dram_tensor("out_x", (N, D), F32, kind="ExternalOutput").ap()
    build(nc, *args, result)
    return run(nc, [arrays], core_ids=[0]).results[0]["out_x"]
```
